# Optimizing a Trainium2 kernel written in Bass

```python
import numpy as np
import jax
import jax.numpy as jnp

def _softmax(x, axis=-1):
    return jax.nn.softmax(x, axis=axis)

def _gelu(x):
    return jax.nn.gelu(x, approximate=True)

def _silu(x):
    return jax.nn.silu(x)

def _sigmoid(x):
    return jax.nn.sigmoid(x)

def _layernorm(x, axis=-1, eps=1e-05):
    m = jnp.mean(x, axis=axis, keepdims=True)
    v = jnp.var(x, axis=axis, keepdims=True)
    return (x - m) / jnp.sqrt(v + eps)

def _scatter_add(tgt, idx, src, axis=0):
    return tgt.at[idx].add(src)

def _segment_sum(src, seg, n):
    return jax.ops.segment_sum(src, seg, n)
kernel_name = 'mk_gnn_preln_d2_gnn_r8_3c738c'

def setup_inputs(seed: int=0):
    np.random.seed(seed)
    _w = jnp.asarray

    def _rec_inputs():
        import jax
        import jax.numpy as jnp
        _gk = jax.random.key(seed)
        x = -0.0001126 + 1 * jax.random.normal(jax.random.fold_in(_gk, 1), (1250, 768), jnp.float32)
        src = jax.random.randint(jax.random.fold_in(_gk, 2), (40000,), 0, 1250, jnp.int32)
        dst = jax.random.randint(jax.random.fold_in(_gk, 3), (40000,), 0, 1250, jnp.int32)
        _o = jnp.argsort(dst, stable=True)
        src = src[_o]
        dst = dst[_o]
        return (x, src, dst)
    x, src, dst = _rec_inputs()

    def _L0_gnn_setup():
        import jax, jax.numpy as jnp
        import numpy as np
        N_NODES = 1250
        N_EDGES = 20000
        NEG_SLOPE = 0.2

        def _gat_layer(x, src, dst, W, a_src, a_dst, bias, concat):
            N = x.shape[0]
            H, C = a_src.shape
            h = (x @ W).reshape(N, H, C)
            al_s = jnp.einsum('nhc,hc->nh', h, a_src)
            al_d = jnp.einsum('nhc,hc->nh', h, a_dst)
            e = jax.nn.leaky_relu(al_s[src] + al_d[dst], NEG_SLOPE)
            m = jax.ops.segment_max(e, dst, num_segments=N)
            ex = jnp.exp(e - m[dst])
            denom = jax.ops.segment_sum(ex, dst, num_segments=N)
            alpha = ex / (denom[dst] + 1e-16)
            msg = h[src] * alpha[:, :, None]
            out = jax.ops.segment_sum(msg, dst, num_segments=N)
            out = out.reshape(N, H * C) if concat else out.mean(axis=1)
            return out + bias
        key = jax.random.key(seed)
        ks = jax.random.split(key, 10)
        in_dim, hid, out_dim, heads = (768, 512, 768, 4)
        x = jax.random.normal(ks[0], (N_NODES, in_dim), dtype=jnp.float32)
        edge_index = jax.random.randint(ks[1], (2, N_EDGES), 0, N_NODES, dtype=jnp.int64)
        g = lambda k, shape, fan: jax.random.normal(k, shape, jnp.float32) / np.sqrt(fan)
        return {'x': x, 'edge_index': edge_index, 'W1': g(ks[2], (in_dim, heads * hid), in_dim), 'att_src1': g(ks[3], (heads, hid), hid), 'att_dst1': g(ks[4], (heads, hid), hid), 'b1': jnp.zeros((heads * hid,), jnp.float32), 'W2': g(ks[5], (heads * hid, out_dim), heads * hid), 'att_src2': g(ks[6], (1, out_dim), out_dim), 'att_dst2': g(ks[7], (1, out_dim), out_dim), 'b2': jnp.zeros((out_dim,), jnp.float32)}
    _L0_gnn_all = _L0_gnn_setup()
    _L0_gnn_in = {k: v for k, v in _L0_gnn_all.items() if k in ('W1', 'att_src1', 'att_dst1', 'b1', 'W2', 'att_src2', 'att_dst2', 'b2')}
    del _L0_gnn_all

    def _L1_gnn_setup():
        import jax, jax.numpy as jnp
        import numpy as np
        N_NODES = 1250
        D = 768
        N_EDGES = 20000

        def gcn_conv(x, W, b, src, dst, n_nodes):
            h = x @ W
            deg = jax.ops.segment_sum(jnp.ones_like(dst, dtype=h.dtype), dst, num_segments=n_nodes)
            dinv = jnp.where(deg > 0, jax.lax.rsqrt(deg), 0.0)
            norm = dinv[src] * dinv[dst]
            msgs = h[src] * norm[:, None]
            out = jax.ops.segment_sum(msgs, dst, num_segments=n_nodes)
            return out + b

        def add_self_loops(edge_index, n_nodes):
            loop = jnp.arange(n_nodes, dtype=edge_index.dtype)
            src = jnp.concatenate([edge_index[0], loop])
            dst = jnp.concatenate([edge_index[1], loop])
            return (src, dst)
        key = jax.random.key(seed)
        k1, k2, k3, k4 = jax.random.split(key, 4)
        x = jax.random.normal(k1, (N_NODES, D), dtype=jnp.float32)
        edge_index = jax.random.randint(k2, (2, N_EDGES), 0, N_NODES, dtype=jnp.int32)
        glorot = float(np.sqrt(6.0 / (D + D)))
        W1 = jax.random.uniform(k3, (D, D), jnp.float32, -glorot, glorot)
        W2 = jax.random.uniform(k4, (D, D), jnp.float32, -glorot, glorot)
        b1 = jnp.zeros((D,), jnp.float32)
        b2 = jnp.zeros((D,), jnp.float32)
        return {'x': x, 'W1': W1, 'b1': b1, 'W2': W2, 'b2': b2, 'edge_index': edge_index}
    _L1_gnn_all = _L1_gnn_setup()
    _L1_gnn_in = {k: v for k, v in _L1_gnn_all.items() if k in ('W1', 'b1', 'W2', 'b2')}
    del _L1_gnn_all
    return {'x': x, 'src': src, 'dst': dst, 'L0_gnn_W1': _L0_gnn_in['W1'], 'L0_gnn_att_src1': _L0_gnn_in['att_src1'], 'L0_gnn_att_dst1': _L0_gnn_in['att_dst1'], 'L0_gnn_b1': _L0_gnn_in['b1'], 'L0_gnn_W2': _L0_gnn_in['W2'], 'L0_gnn_att_src2': _L0_gnn_in['att_src2'], 'L0_gnn_att_dst2': _L0_gnn_in['att_dst2'], 'L0_gnn_b2': _L0_gnn_in['b2'], 'L1_gnn_W1': _L1_gnn_in['W1'], 'L1_gnn_b1': _L1_gnn_in['b1'], 'L1_gnn_W2': _L1_gnn_in['W2'], 'L1_gnn_b2': _L1_gnn_in['b2']}

def reference(x, src, dst, L0_gnn_W1, L0_gnn_att_src1, L0_gnn_att_dst1, L0_gnn_b1, L0_gnn_W2, L0_gnn_att_src2, L0_gnn_att_dst2, L0_gnn_b2, L1_gnn_W1, L1_gnn_b1, L1_gnn_W2, L1_gnn_b2):
    import jax
    import jax.numpy as jnp

    def _L0_gnn_ref(x, edge_index, W1, att_src1, att_dst1, b1, W2, att_src2, att_dst2, b2):
        import jax, jax.numpy as jnp
        import numpy as np
        N_NODES = 1250
        N_EDGES = 20000
        NEG_SLOPE = 0.2

        def _gat_layer(x, src, dst, W, a_src, a_dst, bias, concat):
            N = x.shape[0]
            H, C = a_src.shape
            h = (x @ W).reshape(N, H, C)
            al_s = jnp.einsum('nhc,hc->nh', h, a_src)
            al_d = jnp.einsum('nhc,hc->nh', h, a_dst)
            e = jax.nn.leaky_relu(al_s[src] + al_d[dst], NEG_SLOPE)
            m = jax.ops.segment_max(e, dst, num_segments=N)
            ex = jnp.exp(e - m[dst])
            denom = jax.ops.segment_sum(ex, dst, num_segments=N)
            alpha = ex / (denom[dst] + 1e-16)
            msg = h[src] * alpha[:, :, None]
            out = jax.ops.segment_sum(msg, dst, num_segments=N)
            out = out.reshape(N, H * C) if concat else out.mean(axis=1)
            return out + bias
        N = x.shape[0]
        loops = jnp.arange(N, dtype=edge_index.dtype)
        src = jnp.concatenate([edge_index[0], loops])
        dst = jnp.concatenate([edge_index[1], loops])
        h = jax.nn.elu(_gat_layer(x, src, dst, W1, att_src1, att_dst1, b1, concat=True))
        out = _gat_layer(h, src, dst, W2, att_src2, att_dst2, b2, concat=False)
        return out

    def _L1_gnn_ref(x, W1, b1, W2, b2, edge_index):
        import jax, jax.numpy as jnp
        import numpy as np
        N_NODES = 1250
        D = 768
        N_EDGES = 20000

        def gcn_conv(x, W, b, src, dst, n_nodes):
            h = x @ W
            deg = jax.ops.segment_sum(jnp.ones_like(dst, dtype=h.dtype), dst, num_segments=n_nodes)
            dinv = jnp.where(deg > 0, jax.lax.rsqrt(deg), 0.0)
            norm = dinv[src] * dinv[dst]
            msgs = h[src] * norm[:, None]
            out = jax.ops.segment_sum(msgs, dst, num_segments=n_nodes)
            return out + b

        def add_self_loops(edge_index, n_nodes):
            loop = jnp.arange(n_nodes, dtype=edge_index.dtype)
            src = jnp.concatenate([edge_index[0], loop])
            dst = jnp.concatenate([edge_index[1], loop])
            return (src, dst)
        n = x.shape[0]
        src, dst = add_self_loops(edge_index, n)
        h = gcn_conv(x, W1, b1, src, dst, n)
        h = jax.nn.relu(h)
        out = gcn_conv(h, W2, b2, src, dst, n)
        return out
    edge_index = jnp.stack([src, dst])
    h = jnp.maximum(_layernorm(x, axis=-1), 0.0)
    x = x + _L0_gnn_ref(h, edge_index, L0_gnn_W1, L0_gnn_att_src1, L0_gnn_att_dst1, L0_gnn_b1, L0_gnn_W2, L0_gnn_att_src2, L0_gnn_att_dst2, L0_gnn_b2)
    h = jnp.maximum(_layernorm(x, axis=-1), 0.0)
    x = x + _L1_gnn_ref(h, L1_gnn_W1, L1_gnn_b1, L1_gnn_W2, L1_gnn_b2, edge_index)
    return x

_drawn_inputs = setup_inputs


def setup_inputs(seed=0):
    import zlib

    import numpy as np

    out = dict(_drawn_inputs(seed))
    spreads = {'L0_gnn_b1': (0.0, 0.1),
     'L0_gnn_b2': (0.0, 0.1),
     'L1_gnn_b1': (0.0, 0.1),
     'L1_gnn_b2': (0.0, 0.1)}
    factors = {'L0_gnn_att_src1': 3.901,
     'L0_gnn_att_dst1': 8.0,
     'L0_gnn_att_src2': 8.0,
     'L0_gnn_att_dst2': 44.079}
    for name, (base, spread) in spreads.items():
        noise = np.random.default_rng([zlib.crc32(name.encode()), seed]).standard_normal(out[name].shape)
        drawn = base * np.exp(spread * noise) if base else spread * noise
        out[name] = jnp.asarray(drawn.astype(out[name].dtype))
    for name, factor in factors.items():
        out[name] = (out[name] * factor).astype(out[name].dtype)
    return out
```

```python
import concourse.bass as bass
from concourse import mybir
from contextlib import ExitStack

fp32 = mybir.dt.float32
f32r = mybir.dt.float32r
bf16 = mybir.dt.bfloat16
u16 = mybir.dt.uint16
i32 = mybir.dt.int32
ALU = mybir.AluOpType
ACT = mybir.ActivationFunctionType
AX = mybir.AxisListType

P = 128
N = 1250
D = 768
E = 40000
HEADS, HID = 4, 512
T = (N + P - 1) // P
NP = T * P
LAST = N - (T - 1) * P
KD = D // P
KH = HID // P
EPS = 1e-5
SLOPE = 0.2
FAR = -1e30

EC = 125
NCH = E // EC
EJ = 4
NS = NCH // EJ
EP = NS
WD = 32
NW = NP // WD
WK = WD * T
OH = P + WK
SW = EJ * OH
OSLOTS = 8

CW = 256
CHUNKS = [(c, min(CW, N - c)) for c in range(0, N, CW)]
NC = len(CHUNKS)
G = 2
NG = T // G
HALF = D // 2
AUG = D + 4
AH = AUG // 2
ONE = D - AH


def rows_of(t):
    return P if t < T - 1 else LAST


def build(nc, x, src, dst, W1, as1, ad1, b1, W2, as2, ad2, b2, G1, c1, G2, c2, out):
    keep = ExitStack()

    def pool(stack):
        return (lambda n, s, d: stack.enter_context(nc.sbuf_tensor(n, s, d)),
                lambda n, s: stack.enter_context(nc.psum_tensor(n, s, fp32)),
                lambda n: stack.enter_context(nc.semaphore(n)))

    with keep:
        sb, _, _ = pool(keep)
        ident = sb("ident", [P, P], fp32)
        ones_r = sb("ones_r", [P, P], f32r)
        counts = sb("counts", [P, T, NP], u16)
        dinv = sb("dinv", [P, T], fp32)
        al = sb("al", [P, T, 2 * HEADS], fp32)
        al02 = sb("al02", [P, T, 2 * HEADS], fp32)
        shiftT = sb("shiftT", [2 * T, HEADS, P], fp32)
        h_scratch = nc.dram_tensor("h_scratch", [HEADS, P, T, HID], fp32).ap()
        g_scratch = nc.dram_tensor("g_scratch", [T, P, D], fp32).ap()

        with ExitStack() as st:
            front(nc, pool, st, x, src, dst, W1, as1, ad1, ident, ones_r, counts, al, al02, h_scratch)
        with ExitStack() as st:
            sb, _, _ = pool(st)
            deg = sb("deg", [P, T], fp32)
            stats = sb("stats_n", [P, T, 2, 6], fp32)
            mv = sb("mv_n", [P, T, 2], fp32)
            rows = sb("rows", [P, T, D], fp32)
            with ExitStack() as st2:
                first_layer(nc, pool, st2, W2, b1, as2, ad2, ident, ones_r, counts, deg, al, al02, shiftT, h_scratch, rows)
            with ExitStack() as st2:
                second_layer(nc, pool, st2, x, b2, ident, counts, deg, dinv, al, al02, shiftT, rows, stats, mv)
            with ExitStack() as st2:
                convolutions(nc, pool, st2, G1, c1, G2, c2, counts, dinv, rows, mv, g_scratch, out)


def row_stats(nc, chain, stats, mv, rows, t):
    for k in range(2):
        chain(nc.vector.bn_stats(stats[:, t, k, :], rows[:, t, k * HALF:(k + 1) * HALF]), k == 1)
    chain(nc.vector.bn_aggr(mv[:, t, :], stats[:, t, :, :].rearrange("p k s -> p (k s)")))


def inverse_root(nc, chain, v, root, y, tmp):
    chain(nc.vector.reciprocal(y, root))
    chain(nc.vector.tensor_tensor(tmp, y, y, ALU.mult))
    chain(nc.vector.tensor_tensor(tmp, tmp, v, ALU.mult))
    chain(nc.vector.tensor_scalar(tmp, tmp, -0.5, 1.5, ALU.mult, ALU.add))
    chain(nc.vector.tensor_tensor(y, y, tmp, ALU.mult))


def chain_on(engine, sem):
    n = [0]

    def chain(ins, wait=True):
        ins.then_inc(sem, 1)
        n[0] += 1
        if wait:
            engine.wait_ge(sem, n[0])
    return chain


def front(nc, pool, st, x, src, dst, W1, as1, ad1, ident, ones_r, counts, al, al02, h_scratch):
    sb, pb, sem = pool(st)
    vcol = sb("vcol", [P, KD, 2 * HEADS], fp32)
    xT = [sb("xT_hi", [P, KD, NP], f32r), sb("xT_lo", [P, KD, NP], f32r)]

    with ExitStack() as st_e:
        sbe, _, _ = pool(st_e)
        key = sbe("key", [EC, NCH], fp32)
        low = sbe("low", [EC, NCH], fp32)
        iota = sbe("iota", [EC, NW * WK], u16)
        bounds = sbe("bounds", [1, NW], i32)
        w_st = sbe("w_st", [P, KD, HID], fp32)
        abc = sbe("abc", [P, 2, HID], fp32)
        _, _, seme = pool(st_e)
        w_in = seme("w_in")
        a_in = seme("a_in")

        def load_weights(sp, h):
            for a, vec in enumerate((as1, ad1)):
                sp.dma_start(abc[:, a, :], vec[bass.ds(h, 1), :].to_broadcast([P, HID])).then_inc(a_in, 16)
            sp.dma_start(w_st[:, :, :], W1.rearrange("(k p) n -> p k n", p=P)[:, :, bass.ds(h * HID, HID)]).then_inc(w_in, 16)

        def window(engine, w):
            word = engine.value_load(bounds[0:1, bass.ds(w, 1)], min_val=0, max_val=((NW + 1) * NS << 16) - 1)
            first = nc.s_assert_within(engine.snap(word % 256), 0, NS - 3)
            final = nc.s_assert_within(engine.snap((word // 256) % 256), 2, NS - 1)
            return first, final, nc.s_assert_within(engine.snap(word // 65536), 3, (NW + 1) * NS - 1)

        with ExitStack() as st_a:
            sba, pba, sema = pool(st_a)
            xr = sba("xr", [P, T, D], fp32)
            stats = sba("stats", [P, T, 2, 6], fp32)
            mv = sba("mv", [P, T, 2], fp32)
            ve, root, rstd, nmr, tmp = (sba(n, [P, T], fp32) for n in ("ve", "root", "rstd", "nmr", "tmp"))
            e_i = sba("e_i", [EP, 2, EJ, EC], i32)
            e_f = sba("e_f", [EP, 2, EJ, EC], fp32)
            s_i = sba("s_i", [EC, NCH], i32)
            s_hi = sba("s_hi", [EC, NCH], i32)
            s_lo = sba("s_lo", [EC, NCH], i32)
            d_f = sba("d_f", [EC, NCH], fp32)
            w_i = sba("w_i", [EP, NW], i32)
            w_f = sba("w_f", [EP, 2, NW], fp32)
            c_i = sba("c_i", [EP, 2], i32)
            c_f = sba("c_f", [EP, 2], fp32)
            dmm = sba("dmm", [EP, 2], fp32)
            ov = sba("ov", [EP, NW], fp32)
            cand = sba("cand", [EP, 2, NW], fp32)
            far = sba("far", [NW, 2], fp32)
            wc = sba("wc", [NW, 3], fp32)
            tri = sba("tri", [NW, NW], fp32)
            rowf = sba("rowf", [1, 3, NW], fp32)
            rowi = sba("rowi", [1, 3, NW], i32)
            p_x = [pba("p_x0", [P, 8, P]), pba("p_x1", [P, 8, P])]
            p_e = pba("p_e", [EC, 2, 512])
            p_w = pba("p_w", [NW, 2, EP])
            p_r = pba("p_r", [1, 3, NW])
            x_in = [sema(f"x_in{t}") for t in range(T)]
            e_in = sema("e_in")
            made = sema("made")
            v_step = sema("v_step")
            pad_zero = sema("pad_zero")
            roots = sema("roots")
            var_done = sema("var_done")
            norm_ready = sema("norm_ready")
            h_done = sema("h_done")
            xt_done = sema("xt_done")
            hi_done = sema("hi_done")
            lo_done = sema("lo_done")
            ef_ready = sema("ef_ready")
            et_done = sema("et_done")
            red_ready = sema("red_ready")
            wt_done = sema("wt_done")
            wc_ready = sema("wc_ready")
            wr_done = sema("wr_done")

            with nc.Block() as block:
                @block.sync
                def _(sp):
                    for t in range(T):
                        if t == T - 1:
                            sp.wait_ge(pad_zero, 1)
                        sp.dma_start(xr[0:rows_of(t), t, :], x[t * P:t * P + rows_of(t), :]).then_inc(x_in[t], 16)
                    load_weights(sp, 0)

                @block.gpsimd
                def _(pool_):
                    nc.gpsimd.memset(ident[:, :], 0.0).then_inc(made, 1)
                    nc.gpsimd.memset(tri[:, :], 1.0).then_inc(made, 1)
                    nc.gpsimd.memset(ones_r[:, :].bitcast(fp32), 1.0).then_inc(made, 1)
                    nc.gpsimd.iota(w_i[:, :], pattern=[[WD, NW]], base=0, channel_multiplier=0).then_inc(made, 1)
                    nc.gpsimd.iota(c_i[:, 0:1], pattern=[[0, 1]], base=1, channel_multiplier=1).then_inc(made, 1)
                    nc.gpsimd.iota(c_i[:, 1:2], pattern=[[0, 1]], base=NS, channel_multiplier=-1).then_inc(made, 1)
                    pool_.wait_ge(made, 6)
                    nc.gpsimd.affine_select(out=ident[:, :], in_=ident[:, :], compare_op=ALU.not_equal, fill=1.0,
                                            base=0, pattern=[[-1, P]], channel_multiplier=1).then_inc(made, 1)
                    nc.gpsimd.affine_select(out=tri[:, :], in_=tri[:, :], compare_op=ALU.is_gt, fill=0.0,
                                            base=0, pattern=[[1, NW]], channel_multiplier=-1).then_inc(made, 1)
                    nc.gpsimd.iota(iota[:, :], pattern=[[1, NW * WK]], base=0, channel_multiplier=0).then_inc(made, 1)
                    pool_.wait_ge(norm_ready, 1)
                    for t in range(T):
                        nc.gpsimd.tensor_scalar(xr[:, t, :], xr[:, t, :], rstd[:, t:t + 1], nmr[:, t:t + 1],
                                                ALU.mult, ALU.add).then_inc(h_done, 1)
                    pool_.wait_ge(made, 9)

                @block.scalar
                def _(act):
                    act.dma_start(e_i[:, 0, :, :], src.rearrange("(p j e) -> p j e", j=EJ, e=EC)).then_inc(e_in, 16)
                    act.dma_start(e_i[:, 1, :, :], dst.rearrange("(p j e) -> p j e", j=EJ, e=EC)).then_inc(e_in, 16)
                    act.wait_ge(var_done, 1)
                    nc.scalar.activation(root[:, :], ve[:, :], ACT.Sqrt).then_inc(roots, 1)
                    for t in range(T):
                        act.wait_ge(xt_done, t + 1)
                        nc.scalar.activation(xT[0][:, :, t * P:(t + 1) * P], p_x[t % 2][:, 0:KD, :], ACT.Relu).then_inc(hi_done, 1)

                @block.tensor
                def _(pe):
                    pe.wait_ge(made, 8)
                    pe.wait_ge(ef_ready, 1)
                    for a in range(2):
                        for j in range(EJ):
                            last = nc.tensor.transpose(p_e[:, a, j * EP:(j + 1) * EP], e_f[:, a, j, :], ident[0:EP, 0:EP])
                    last.then_inc(et_done, 1)
                    pe.wait_ge(red_ready, 1)
                    for a in range(2):
                        last = nc.tensor.matmul(p_w[:, a, :], cand[:, a, :], ident[0:EP, 0:EP], start=True, stop=True)
                    last.then_inc(wt_done, 1)
                    pe.wait_ge(wc_ready, 1)
                    for a in range(3):
                        last = nc.tensor.matmul(p_r[:, a, :], wc[:, a:a + 1], ident[0:NW, 0:NW] if a < 2 else tri[:, :],
                                                start=True, stop=True)
                    last.then_inc(wr_done, 1)
                    for t in range(T):
                        pe.wait_ge(h_done, t + 1)
                        if t >= 2:
                            pe.wait_ge(lo_done, t - 1)
                        for k in range(KD):
                            last = nc.tensor.transpose(p_x[t % 2][:, k, :], xr[:, t, k * P:(k + 1) * P], ident[:, :])
                        last.then_inc(xt_done, 1)

                @block.vector
                def _(dve):
                    chain = chain_on(dve, v_step)
                    nc.vector.memset(xr[96:P, T - 1, :], 0.0).then_inc(pad_zero, 1)
                    dve.wait_ge(e_in, 32)
                    nc.vector.tensor_copy(e_f[:, :, :, :], e_i[:, :, :, :]).then_inc(ef_ready, 1)
                    dve.wait_ge(ef_ready, 1)
                    span = e_f[:, 1, :, :].rearrange("p j e -> p (j e)")
                    chain(nc.vector.tensor_reduce(dmm[:, 0:1], span, AX.X, ALU.min), False)
                    chain(nc.vector.tensor_reduce(dmm[:, 1:2], span, AX.X, ALU.max), False)
                    dve.wait_ge(made, 6)
                    chain(nc.vector.tensor_copy(w_f[:, 0, :], w_i[:, :]), False)
                    chain(nc.vector.tensor_scalar(w_f[:, 1, :], w_i[:, :], float(WD - 1), None, ALU.add), False)
                    chain(nc.vector.tensor_copy(c_f[:, :], c_i[:, :]))
                    chain(nc.vector.tensor_scalar(ov[:, :], w_f[:, 0, :], dmm[:, 1:2], None, ALU.is_le))
                    chain(nc.vector.scalar_tensor_tensor(out=ov[:, :], in0=w_f[:, 1, :], scalar=dmm[:, 0:1], in1=ov[:, :],
                                                         op0=ALU.is_ge, op1=ALU.mult))
                    for a in range(2):
                        ins = nc.vector.tensor_scalar(cand[:, a, :], ov[:, :], c_f[:, a:a + 1], None, ALU.mult)
                        ins.then_inc(red_ready, 1) if a else chain(ins)
                    dve.wait_ge(wt_done, 1)
                    chain(nc.vector.tensor_reduce(far[:, :], p_w[:, :, :], AX.X, ALU.max))
                    chain(nc.vector.tensor_scalar(wc[:, 0:1], far[:, 1:2], -1.0, float(NS), ALU.mult, ALU.add))
                    chain(nc.vector.tensor_scalar(wc[:, 0:1], wc[:, 0:1], float(NS - 3), None, ALU.min))
                    chain(nc.vector.tensor_scalar(wc[:, 2:3], wc[:, 0:1], 2.0, None, ALU.add))
                    chain(nc.vector.scalar_tensor_tensor(out=wc[:, 1:2], in0=far[:, 0:1], scalar=-1.0, in1=wc[:, 2:3],
                                                         op0=ALU.add, op1=ALU.max))
                    nc.vector.scalar_tensor_tensor(out=wc[:, 2:3], in0=wc[:, 1:2], scalar=1.0, in1=wc[:, 0:1],
                                                   op0=ALU.add, op1=ALU.subtract).then_inc(wc_ready, 1)
                    dve.wait_ge(wr_done, 1)
                    chain(nc.vector.tensor_copy(rowf[:, :, :], p_r[:, :, :]))
                    chain(nc.vector.tensor_copy(rowi[:, 0:2, :], rowf[:, 0:2, :]))
                    chain(nc.vector.scalar_tensor_tensor(out=rowi[:, 2, :], in0=rowf[:, 2, :], scalar=float(NS), in1=rowf[:, 0, :],
                                                         op0=ALU.add, op1=ALU.subtract))
                    for a in (1, 2):
                        chain(nc.vector.tensor_scalar(rowi[:, a, :], rowi[:, a, :], 8 * a, None, ALU.logical_shift_left))
                    chain(nc.vector.tensor_tensor(bounds[:, :], rowi[:, 0, :], rowi[:, 1, :], ALU.bitwise_or))
                    chain(nc.vector.tensor_tensor(bounds[:, :], bounds[:, :], rowi[:, 2, :], ALU.bitwise_or), False)
                    dve.wait_ge(et_done, 1)
                    chain(nc.vector.tensor_copy(s_i[:, :].rearrange("e (p j) -> e j p", j=EJ),
                                                p_e[:, 0, 0:NCH].rearrange("e (j p) -> e j p", j=EJ)), False)
                    chain(nc.vector.tensor_scalar(d_f[:, :].rearrange("e (p j) -> e j p", j=EJ),
                                                  p_e[:, 1, 0:NCH].rearrange("e (j p) -> e j p", j=EJ),
                                                  float(T), None, ALU.mult))
                    chain(nc.vector.tensor_scalar(s_hi[:, :], s_i[:, :], 7, None, ALU.logical_shift_right), False)
                    chain(nc.vector.tensor_scalar(s_lo[:, :], s_i[:, :], P - 1, None, ALU.bitwise_and))
                    chain(nc.vector.tensor_tensor(key[:, :], d_f[:, :], s_hi[:, :], ALU.add), False)
                    chain(nc.vector.tensor_copy(low[:, :], s_lo[:, :]))
                    for t in range(T):
                        dve.wait_ge(x_in[t], 16)
                        row_stats(nc, chain, stats, mv, xr, t)
                    nc.vector.tensor_scalar(ve[:, :], mv[:, :, 1], EPS, None, ALU.add).then_inc(var_done, 1)
                    dve.wait_ge(roots, 1)
                    inverse_root(nc, chain, ve[:, :], root[:, :], rstd[:, :], tmp[:, :])
                    nc.vector.scalar_tensor_tensor(out=nmr[:, :], in0=mv[:, :, 0], scalar=-1.0, in1=rstd[:, :],
                                                   op0=ALU.mult, op1=ALU.mult).then_inc(norm_ready, 1)
                    for t in range(T):
                        dve.wait_ge(hi_done, t + 1)
                        hi = xT[0][:, :, t * P:(t + 1) * P].bitcast(fp32)
                        nc.vector.scalar_tensor_tensor(out=xT[1][:, :, t * P:(t + 1) * P], in0=p_x[t % 2][:, 0:KD, :], scalar=0.0,
                                                       in1=hi, op0=ALU.max, op1=ALU.subtract).then_inc(lo_done, 1)

        with ExitStack() as st_b:
            sbb, pbb, semb = pool(st_b)
            w = [sbb("w_hi", [P, KD, HID], f32r), sbb("w_lo", [P, KD, HID], f32r)]
            vh = sbb("vh", [P, KD, 2], fp32)
            junk = sbb("junk", [P, 2, HID], fp32)
            mark = sbb("mark", [1, T], fp32)
            hot = sbb("hot", [EC, OSLOTS * SW], bf16)
            stage = sbb("stage", [P, 2, HID], fp32)
            p_c = [pbb("p_c0", [P, 512]), pbb("p_c1", [P, 512])]
            p_h = [pbb("p_h0", [P, HID]), pbb("p_h1", [P, HID])]
            whi_done = semb("whi_done")
            wlo_done = semb("wlo_done")
            v_done = semb("v_done")
            v_copied = semb("v_copied")
            hot_ready = semb("hot_ready")
            hot_used = semb("hot_used")
            win_ready = semb("win_ready")
            win_out = semb("win_out")
            h_ready = semb("h_ready")
            h_out = semb("h_out")
            spilled = [semb("spilled0"), semb("spilled1")]

            with nc.Block() as block:
                @block.sync
                def _(sp):
                    def spill(h, t):
                        sp.wait_ge(h_out, h * T + t + 3)
                        sp.dma_start(h_scratch[bass.ds(h, 1), :, t, :].rearrange("a p c -> p (a c)"),
                                     stage[:, t % 2, :]).then_inc(spilled[t % 2], 16)

                    for j in range(2):
                        sp.sem_inc(spilled[j], 16)
                    with sp.Fori(0, HEADS - 1) as h:
                        for t in range(T):
                            if t == KD + 1:
                                sp.wait_ge(v_done, h * (2 * KD) + 2 * KD + 1)
                                load_weights(sp, h + 1)
                            spill(h, t)
                    for t in range(T):
                        spill(HEADS - 1, t)
                    for j in range(2):
                        sp.wait_ge(spilled[j], 16 + 16 * (HEADS * T // 2))

                @block.scalar
                def _(act):
                    act.sem_inc(win_out, 2)
                    act.sem_inc(h_out, 2)
                    with act.Fori(0, HEADS) as h:
                        act.wait_ge(w_in, h * 16 + 16)
                        for k in range(KD):
                            nc.scalar.activation(w[0][:, k, :], w_st[:, k, :], ACT.Copy).then_inc(whi_done, 1)
                        for t in range(T):
                            act.wait_ge(spilled[t % 2], h * (8 * T) + 16 * (t // 2) + 16)
                            act.wait_ge(h_ready, h * T + t + 1)
                            nc.scalar.activation(stage[:, t % 2, :], p_h[t % 2][:, :], ACT.Copy).then_inc(h_out, 1)
                            first, final, base = window(act, h * T + t)
                            act.wait_ge(hot_used, act.snap(base + final + OSLOTS, min_val=NS, max_val=(NW + 1) * NS + OSLOTS))
                            nc.scalar.activation(mark[:, t:t + 1], p_c[t % 2][0:1, 0:1], ACT.Copy).then_inc(win_ready, 1)
                            act.wait_ge(win_ready, h * T + t + 1)
                            nc.scalar.activation(counts[:, :, bass.ds(h * (T * WD) + t * WD, WD)],
                                                 p_c[t % 2][:, 0:WK].rearrange("p (d s) -> p s d", s=T),
                                                 ACT.Copy).then_inc(win_out, 1)

                @block.vector
                def _(dve):
                    dve.sem_inc(hot_ready, NS - 1)
                    dve.sem_inc(v_done, 1)
                    dve.sem_inc(v_copied, 1)
                    with dve.Fori(0, HEADS) as h:
                        for k in range(KD):
                            dve.wait_ge(whi_done, h * KD + k + 1)
                            nc.vector.tensor_tensor(w[1][:, k, :], w_st[:, k, :], w[0][:, k, :].bitcast(fp32),
                                                    ALU.subtract).then_inc(wlo_done, 1)
                        dve.wait_ge(a_in, h * 32 + 32)
                        dve.wait_ge(v_copied, h * 2 + 1)
                        for t in range(T):
                            first, final, base = window(dve, h * T + t)
                            keys = iota[:, bass.ds(h * (T * WK) + t * WK, WK)]

                            def span(s):
                                nth = dve.snap(base + s, min_val=NS, max_val=(NW + 1) * NS - 1)
                                slot = dve.snap((nth % OSLOTS) * SW, min_val=0, max_val=(OSLOTS - 1) * SW)
                                col = dve.snap(s * EJ, min_val=0, max_val=NCH - EJ)
                                part = hot[:, bass.ds(slot, SW)]
                                lows, span_keys = low[:, bass.ds(col, EJ)], key[:, bass.ds(col, EJ)]
                                dve.wait_ge(hot_used, nth)
                                for j in range(EJ):
                                    nc.vector.tensor_scalar(part[:, j * OH:j * OH + P], iota[:, 0:P], lows[:, j:j + 1], None,
                                                            ALU.is_equal)
                                    last = nc.vector.tensor_scalar(part[:, j * OH + P:(j + 1) * OH], keys, span_keys[:, j:j + 1],
                                                                   None, ALU.is_equal)
                                last.then_inc(hot_ready, 1)

                            span(first)
                            with dve.Fori(first + 1, final) as s:
                                span(s)
                            span(final)
                            if t < KD:
                                for a in range(2):
                                    if t >= 1:
                                        dve.wait_ge(v_done, h * (2 * KD) + 2 * (t - 1) + a + 2)
                                    nc.vector.tensor_tensor_reduce(
                                        out=junk[:, a, :], in0=w_st[:, t, :], in1=abc[:, a, :], scale=1.0, scalar=0.0,
                                        op0=ALU.mult, op1=ALU.add, accum_out=vh[:, t, a:a + 1]).then_inc(v_done, 1)
                        dve.wait_ge(v_done, h * (2 * KD) + 2 * KD + 1)
                        for a in range(2):
                            nc.vector.tensor_copy(vcol[:, :, bass.ds(h + a * HEADS, 1)], vh[:, :, a:a + 1]).then_inc(v_copied, 1)

                @block.tensor
                def _(pe):
                    pe.sem_inc(hot_used, NS - 1 + OSLOTS)
                    with pe.Fori(0, HEADS) as h:
                        for t in range(T):
                            pe.wait_ge(h_out, h * T + t + 1)
                            n = 0
                            for k in range(KD):
                                if t == 0:
                                    pe.wait_ge(wlo_done, h * KD + k + 1)
                                for a, b in ((0, 0), (0, 1), (1, 0)):
                                    last = nc.tensor.matmul(p_h[t % 2][:, :], xT[a][:, k, t * P:(t + 1) * P], w[b][:, k, :],
                                                            start=n == 0, stop=n == 3 * KD - 1)
                                    n += 1
                            last.then_inc(h_ready, 1)

                            first, final, base = window(pe, h * T + t)

                            def span(s, start, stop):
                                nth = pe.snap(base + s, min_val=NS, max_val=(NW + 1) * NS - 1)
                                slot = pe.snap((nth % OSLOTS) * SW, min_val=0, max_val=(OSLOTS - 1) * SW)
                                part = hot[:, bass.ds(slot, SW)]
                                pe.wait_ge(hot_ready, nth)
                                for j in range(EJ):
                                    last = nc.tensor.matmul(p_c[t % 2][:, 0:WK], part[:, j * OH:j * OH + P],
                                                            part[:, j * OH + P:(j + 1) * OH], start=start and j == 0,
                                                            stop=stop and j == EJ - 1)
                                return last.then_inc(hot_used, 1)

                            pe.wait_ge(win_out, h * T + t + 1)
                            span(first, True, False)
                            with pe.Fori(first + 1, final) as s:
                                span(s, False, False)
                            span(final, False, True)

    with ExitStack() as st_c:
        sbc, pbc, semc = pool(st_c)
        vr = [sbc("v_hi", [P, KD, 2 * HEADS], f32r), sbc("v_lo", [P, KD, 2 * HEADS], f32r)]
        p_al = pbc("p_al", [P, T, 2 * HEADS])
        v_step = semc("c_step")
        vhi = semc("vhi")
        vlo = semc("vlo")
        al_done = semc("al_done")
        with nc.Block() as block:
            @block.scalar
            def _(act):
                nc.scalar.activation(vr[0][:, :, :], vcol[:, :, :], ACT.Copy).then_inc(vhi, 1)

            @block.tensor
            def _(pe):
                pe.wait_ge(vlo, 1)
                for t in range(T):
                    n = 0
                    for k in range(KD):
                        for a, b in ((0, 0), (0, 1), (1, 0)):
                            last = nc.tensor.matmul(p_al[:, t, :], xT[a][:, k, t * P:(t + 1) * P], vr[b][:, k, :],
                                                    start=n == 0, stop=n == 3 * KD - 1)
                            n += 1
                last.then_inc(al_done, 1)

            @block.vector
            def _(dve):
                chain = chain_on(dve, v_step)
                for t in range(T):
                    blk = counts[:, t, t * P:(t + 1) * P]
                    chain(nc.vector.tensor_tensor(blk, blk, ident[:, :], ALU.add), False)
                dve.wait_ge(vhi, 1)
                nc.vector.tensor_tensor(vr[1][:, :, :], vcol[:, :, :], vr[0][:, :, :].bitcast(fp32),
                                        ALU.subtract).then_inc(vlo, 1)
                dve.wait_ge(al_done, 1)
                chain(nc.vector.tensor_copy(al[:, :, :], p_al[:, :, :]))
                chain(nc.vector.tensor_scalar(al02[:, :, :], al[:, :, :], SLOPE, None, ALU.mult))


def shifts(nc, pool, heads, ident, counts, al, al02, shiftT, tag, on_sync=None, on_scalar=None, on_gpsimd=None,
           on_tensor=None, on_vector=None):
    with ExitStack() as st:
        sb, pb, sem = pool(st)
        mask = sb("mask" + tag, [P, T, NP], bf16)
        top = sb("top" + tag, [P, 2, NP], fp32)
        amax = sb("amax" + tag, [P, T, heads], fp32)
        peak = sb("peak" + tag, [P, T, heads], fp32)
        m = sb("m" + tag, [P, T, heads], fp32)
        shift = sb("shift" + tag, [P, heads, 2, T], fp32)
        p_t = pb("p_t" + tag, [P, 12, P])
        p_s = pb("p_s" + tag, [2 * T, heads, P])
        v_step = sem("s_step" + tag)
        top_ready = sem("top_ready" + tag)
        top_t = sem("top_t" + tag)
        reduced = sem("reduced" + tag)
        shift_ready = sem("shift_ready" + tag)
        shift_t = sem("shift_t" + tag)
        with nc.Block() as block:
            if on_sync:
                block.sync(on_sync)
            if on_scalar:
                block.scalar(on_scalar)
            if on_gpsimd:
                block.gpsimd(on_gpsimd)

            @block.tensor
            def _(pe):
                for h in range(heads):
                    if on_tensor:
                        on_tensor(pe, h)
                    pe.wait_ge(top_ready, h + 1)
                    if h >= 1:
                        pe.wait_ge(reduced, h)
                    for t in range(T):
                        last = nc.tensor.transpose(p_t[:, t, :], top[:, h % 2, t * P:(t + 1) * P], ident[:, :])
                    last.then_inc(top_t, 1)
                pe.wait_ge(shift_ready, 2)
                for h in range(heads):
                    last = nc.tensor.matmul(p_s[:, h, :], shift[:, h, :, :].rearrange("p a t -> p (a t)"), ident[:, :],
                                            start=True, stop=True)
                last.then_inc(shift_t, 1)

            @block.vector
            def _(dve):
                chain = chain_on(dve, v_step)
                chain(nc.vector.tensor_scalar(mask[:, :, :], counts[:, :, :], 0.0, FAR, ALU.is_equal, ALU.mult))

                def take(h):
                    dve.wait_ge(top_t, h + 1)
                    nc.vector.tensor_reduce(amax[:, :, h], p_t[:, 0:T, :], AX.X, ALU.max).then_inc(reduced, 1)

                for h in range(heads):
                    acc = top[:, h % 2, :]
                    chain(nc.vector.tensor_scalar(acc, mask[:, 0, :], al[:, 0, h:h + 1], None, ALU.add))
                    for t in range(1, T):
                        ins = nc.vector.scalar_tensor_tensor(out=acc, in0=mask[:, t, :], scalar=al[:, t, h:h + 1], in1=acc,
                                                             op0=ALU.add, op1=ALU.max)
                        ins.then_inc(top_ready, 1) if t == T - 1 else chain(ins)
                    if h >= 1:
                        take(h - 1)
                take(heads - 1)
                dve.wait_ge(reduced, heads)
                d_al, d_al02 = (v[:, :, HEADS:HEADS + heads] for v in (al, al02))
                chain(nc.vector.tensor_tensor(peak[:, :, :], amax[:, :, :], d_al, ALU.add))
                chain(nc.vector.scalar_tensor_tensor(out=m[:, :, :], in0=peak[:, :, :], scalar=SLOPE, in1=peak[:, :, :],
                                                     op0=ALU.mult, op1=ALU.max))
                for a, v in enumerate((d_al, d_al02)):
                    ins = nc.vector.tensor_tensor(shift[:, :, a, :].rearrange("p h t -> p t h"), v, m[:, :, :], ALU.subtract)
                    ins.then_inc(shift_ready, 1)
                dve.wait_ge(shift_t, 1)
                chain(nc.vector.tensor_copy(shiftT[:, 0:heads, :], p_s[:, :, :]))
                if on_vector:
                    on_vector(dve)


class Weights:

    def __init__(self, pool, st, tag):
        sb, pb, sem = pool(st)
        self.e = sb("e" + tag, [P, 2, 2, G, CW], fp32)
        self.pf = sb("pf" + tag, [P, 2, G, CW], fp32)
        self.ring = [sb("ring_hi" + tag, [P, NG, G, CW], f32r), sb("ring_lo" + tag, [P, NG, G, CW], f32r)]
        self.p_shift = pb("p_shift" + tag, [P, 2, CW])
        self.shift_in = sem("shift_in" + tag)
        self.e_ready = sem("e_ready" + tag)
        self.e_max = sem("e_max" + tag)
        self.pf_ready = sem("pf_ready" + tag)
        self.hi_ready = sem("hi_ready" + tag)
        self.lo_ready = sem("lo_ready" + tag)
        self.used = sem("used" + tag)

    def broadcast(self, nc, pe, ident, shift_rows, q, c):
        pe.wait_ge(self.e_ready, q * NG + 1)
        for a in range(2):
            for dt in range(CW // P):
                row = a * T + c * (CW // P) + dt
                last = nc.tensor.matmul(self.p_shift[:, a, dt * P:(dt + 1) * P],
                                        ident[0:2 * T, row:row + 1].to_broadcast([2 * T, P]), shift_rows,
                                        start=True, stop=True)
        last.then_inc(self.shift_in, 1)

    def exps(self, nc, act, scores, q, c, g):
        n = CHUNKS[c][1]
        local = c * NG + g
        if g == 0:
            act.wait_ge(self.shift_in, q + 1)
        act.wait_ge(self.pf_ready, q * NG + g + (2 if local == 0 else 1))
        for i in range(G):
            for a in range(2):
                last = nc.scalar.activation(self.e[:, local % 2, a, i, 0:n], self.p_shift[:, a, 0:n], ACT.Exp,
                                            bias=scores[a][:, g * G + i:g * G + i + 1])
        last.then_inc(self.e_ready, 1)

    def hi(self, nc, act, q, c, g):
        n = CHUNKS[c][1]
        act.wait_ge(self.pf_ready, q * NG + g + 3)
        act.wait_ge(self.used, q * NG + g + 1)
        nc.scalar.activation(self.ring[0][:, g, :, 0:n], self.pf[:, (c * NG + g) % 2, :, 0:n], ACT.Copy)\
            .then_inc(self.hi_ready, 1)

    def weigh(self, nc, dve, counts, q, c, g):
        d0, n = CHUNKS[c]
        local = c * NG + g
        e = self.e[:, local % 2, :, :, 0:n]
        dve.wait_ge(self.e_ready, q * NG + g + 2)
        nc.vector.tensor_tensor(e[:, 0], e[:, 0], e[:, 1], ALU.max).then_inc(self.e_max, 1)
        dve.wait_ge(self.e_max, q * NG + g + 1)
        nc.vector.scalar_tensor_tensor(out=self.pf[:, local % 2, :, 0:n], in0=e[:, 0], scalar=1.0,
                                       in1=counts[:, g * G:(g + 1) * G, d0:d0 + n], op0=ALU.min, op1=ALU.mult)\
            .then_inc(self.pf_ready, 1)

    def lo(self, nc, dve, q, c, g):
        n = CHUNKS[c][1]
        dve.wait_ge(self.hi_ready, q * NG + g + 1)
        nc.vector.tensor_tensor(self.ring[1][:, g, :, 0:n], self.pf[:, (c * NG + g) % 2, :, 0:n],
                                self.ring[0][:, g, :, 0:n].bitcast(fp32), ALU.subtract).then_inc(self.lo_ready, 1)


def first_layer(nc, pool, st, W2, b1, as2, ad2, ident, ones_r, counts, deg, al, al02, shiftT, h_scratch, rows):
    sb, pb, sem = pool(st)
    hs = sb("hs1", [P, T, 2, HID], f32r)
    h_in = [sem(f"h_in{t}") for t in range(T)]

    def load_rows(sp):
        for t in range(T):
            sp.dma_start(hs[:, t, 1, :].bitcast(fp32), h_scratch[0, :, t, :]).then_inc(h_in[t], 16)

    with ExitStack() as st_d:
        sbd, pbd, semd = pool(st_d)
        p_d = pbd("p_d", [P, T, 2])
        cf = sbd("counts_f", [P, 2, NP], fp32)
        cf_ready, deg_done, deg_ready = semd("cf_ready"), semd("deg_done"), semd("deg_ready")

        def copy_counts(act):
            for s in range(T):
                if s >= 2:
                    act.wait_ge(deg_done, s - 1)
                nc.scalar.activation(cf[:, s % 2, :], counts[:, s, :], ACT.Copy).then_inc(cf_ready, 1)

        def degrees(pe, h):
            per_head = -(-T // HEADS)
            for s in range(h * per_head, min(T, (h + 1) * per_head)):
                pe.wait_ge(cf_ready, s + 1)
                for t in range(T):
                    last = nc.tensor.matmul(p_d[:, t, 0:1], cf[:, s % 2, t * P:(t + 1) * P], ones_r[:, 0:1].bitcast(fp32),
                                            start=s + t == 0, stop=s + t == 2 * (T - 1))
                last.then_inc(deg_done, 1)

        def keep_degrees(dve):
            dve.wait_ge(deg_done, T)
            nc.vector.tensor_copy(deg[:, :], p_d[:, :, 0]).then_inc(deg_ready, 1)
            dve.wait_ge(deg_ready, 1)

        shifts(nc, pool, HEADS, ident, counts, al, al02, shiftT, "one", load_rows, copy_counts, None, degrees, keep_degrees)

    wt = Weights(pool, st, "1")
    w_st = sb("w2_st", [P, KH, D], fp32)
    w = [sb("w2_hi", [P, KH, D], f32r), sb("w2_lo", [P, KH, D], f32r)]
    oT = [sb("oT_hi", [P, KH, CW], f32r), sb("oT_lo", [P, KH, CW], f32r)]
    rden = sb("rden", [P, CW], fp32)
    z = sb("z", [P, KH, CW], fp32)
    neg = sb("neg", [P, KH, CW], fp32)
    pos = sb("pos", [P, KH, CW], fp32)
    bcol = sb("bcol", [P, HEADS * KH], fp32)
    al_h = sb("al_h", [P, 2, T], fp32)
    shift_h = sb("shift_h", [2 * T, P], fp32)
    head_ready = sem("head_ready")
    p_a = pb("p_a1", [P, KH, 512])
    p_den = pb("p_den", [P, 512])
    p_g = [pb("p_g0", [P, 512]), pb("p_g1", [P, 512])]
    hhi_done, hlo_done = sem("hhi_done"), sem("hlo_done")
    w_in, whi_done, wlo_done, b_in = sem("w2_in"), sem("w2hi_done"), sem("w2lo_done"), sem("b1_in")
    rden_done = sem("rden_done")
    z_done = sem("z_done")
    neg_done, pos_done, exp_done, o_done = sem("neg_done"), sem("pos_done"), sem("exp_done"), sem("o_done")
    ohi_done, olo_done = sem("ohi_done"), sem("olo_done")
    g_ready = sem("g_ready")
    g_out = sem("g_out")
    zeroed = sem("zeroed")
    abc = sb("a2bc", [P, 2, D], fp32)
    junk = sb("junk2", [P, 2, D], fp32)
    a_in, scored = sem("a2_in"), sem("scored")
    NB = CW // P * 2

    def before(h, c, k):
        if c >= k:
            return h, c - k
        return None if isinstance(h, int) and h == 0 else (h - 1, c - k + NC)

    def is_final(h):
        return isinstance(h, int) and h == HEADS - 1

    with nc.Block() as block:
        @block.sync
        def _(sp):
            sp.dma_start(bcol[:, :], b1.rearrange("(f p) -> p f", p=P), allow_slow_non_contiguous=True).then_inc(b_in, 16)
            for a, vec in enumerate((as2, ad2)):
                sp.dma_start(abc[:, a, :], vec.to_broadcast([P, D])).then_inc(a_in, 16)
            with sp.Fori(1, HEADS) as h:
                for t in range(T):
                    sp.wait_ge(wt.used, h * (NC * NG) + (t // G + 1))
                    sp.dma_start(hs[:, t, 1, :].bitcast(fp32), h_scratch[bass.ds(h, 1), :, t, :].rearrange("a p c -> p (a c)"))\
                        .then_inc(h_in[t], 16)

        @block.gpsimd
        def _(pool_):
            nc.gpsimd.memset(rows[:, :, :], 0.0).then_inc(zeroed, 1)
            W2v = W2.rearrange("(h k p) n -> p h k n", p=P, h=HEADS)
            with pool_.Fori(0, HEADS) as h:
                pool_.wait_ge(wlo_done, h * KH + 1)
                pool_.dma_start(w_st[:, :, :], W2v[:, bass.ds(h, 1), :, :].rearrange("p a k n -> p (a k) n")).then_inc(w_in, 16)

        @block.scalar
        def _(act):
            def split_rows(h, g):
                for t in range(g * G, (g + 1) * G):
                    act.wait_ge(h_in[t], h * 16 + 16)
                    nc.scalar.activation(hs[:, t, 0, :], hs[:, t, 1, :].bitcast(fp32), ACT.Copy).then_inc(hhi_done, 1)

            def split_weights(h):
                act.wait_ge(w_in, h * 16 + 16)
                act.wait_ge(g_out, h * (NC * NB) + 2)
                for k in range(KH):
                    nc.scalar.activation(w[0][:, k, :], w_st[:, k, :], ACT.Copy).then_inc(whi_done, 1)

            def elu_exp(h, c):
                n = CHUNKS[c][1]
                act.wait_ge(neg_done, (h * NC + c + 1) * KH)
                nc.scalar.activation(neg[:, :, 0:n], neg[:, :, 0:n], ACT.Exp).then_inc(exp_done, 1)

            def elu_hi(h, c):
                n = CHUNKS[c][1]
                act.wait_ge(o_done, h * NC + c + 1)
                nc.scalar.activation(oT[0][:, :, 0:n], z[:, :, 0:n], ACT.Copy).then_inc(ohi_done, 1)

            def head(h):
                for a, scores in enumerate((al, al02)):
                    nc.scalar.activation(al_h[:, a, :], scores[:, :, bass.ds(h, 1)].rearrange("p t a -> p (t a)"),
                                         ACT.Copy).then_inc(head_ready, 1)
                nc.scalar.activation(shift_h[:, :], shiftT[:, bass.ds(h, 1), :].rearrange("r a p -> r (a p)"),
                                     ACT.Copy).then_inc(head_ready, 1)
                act.wait_ge(head_ready, h * 3 + 3)
                scores = al_h[:, 0, :], al_h[:, 1, :]
                for c in range(NC):
                    q, last = h * NC + c, before(h, c, 1)
                    for g in range(NG):
                        wt.exps(nc, act, scores, q, c, g)
                        if g >= 1:
                            wt.hi(nc, act, q, c, g - 1)
                        if c == 0 and 1 <= g <= 2:
                            split_rows(h, g - 1)
                    if c == 0:
                        split_rows(h, 2)
                    if last:
                        elu_exp(*last)
                    if c == 0:
                        split_rows(h, 3)
                    wt.hi(nc, act, q, c, NG - 1)
                    if c == 0:
                        split_rows(h, 4)
                    if last:
                        elu_hi(*last)
                    if c == 1:
                        split_weights(h)

            head(0)
            with act.Fori(1, HEADS - 1) as h:
                head(h)
            head(HEADS - 1)
            elu_exp(HEADS - 1, NC - 1)
            elu_hi(HEADS - 1, NC - 1)

        @block.vector
        def _(dve):
            dve.sem_inc(wt.pf_ready, 2)
            dve.sem_inc(wlo_done, 1)
            dve.sem_inc(z_done, 1)
            dve.sem_inc(g_out, 2)
            dve.wait_ge(b_in, 16)
            dve.wait_ge(zeroed, 1)

            def split_rows(h, g):
                for t in range(g * G, (g + 1) * G):
                    dve.wait_ge(hhi_done, h * T + t + 1)
                    nc.vector.tensor_tensor(hs[:, t, 1, :], hs[:, t, 1, :].bitcast(fp32), hs[:, t, 0, :].bitcast(fp32),
                                            ALU.subtract).then_inc(hlo_done, 1)

            def split_weights(h):
                for k in range(KH):
                    dve.wait_ge(whi_done, h * KH + k + 1)
                    nc.vector.tensor_tensor(w[1][:, k, :], w_st[:, k, :], w[0][:, k, :].bitcast(fp32),
                                            ALU.subtract).then_inc(wlo_done, 1)

            def normalize(h, c):
                n = CHUNKS[c][1]
                q = h * NC + c
                dve.wait_ge(wt.used, (q + 2) * NG)
                nc.vector.reciprocal(rden[:, 0:n], p_den[:, 0:n]).then_inc(rden_done, 1)
                dve.wait_ge(rden_done, q + 1)
                for f in range(KH):
                    last = nc.vector.tensor_tensor(z[:, f, 0:n], p_a[:, f, 0:n], rden[:, 0:n], ALU.mult)
                last.then_inc(z_done, 1)

            def elu_in(h, c):
                n = CHUNKS[c][1]
                dve.wait_ge(z_done, h * NC + c + 2)
                for f in range(KH):
                    bias = bcol[:, bass.ds(h * KH + f, 1)]
                    nc.vector.tensor_scalar(neg[:, f, 0:n], z[:, f, 0:n], bias, 0.0, ALU.add, ALU.min).then_inc(neg_done, 1)
                for f in range(KH):
                    bias = bcol[:, bass.ds(h * KH + f, 1)]
                    nc.vector.tensor_scalar(pos[:, f, 0:n], z[:, f, 0:n], bias, 0.0, ALU.add, ALU.max).then_inc(pos_done, 1)

            def elu_out(h, c):
                n = CHUNKS[c][1]
                q = h * NC + c
                dve.wait_ge(exp_done, q + 1)
                dve.wait_ge(pos_done, (q + 1) * KH)
                nc.vector.scalar_tensor_tensor(out=z[:, :, 0:n], in0=neg[:, :, 0:n], scalar=-1.0, in1=pos[:, :, 0:n],
                                               op0=ALU.add, op1=ALU.add).then_inc(o_done, 1)

            def elu_lo(h, c):
                n = CHUNKS[c][1]
                q = h * NC + c
                dve.wait_ge(ohi_done, q + 1)
                nc.vector.tensor_tensor(oT[1][:, :, 0:n], z[:, :, 0:n], oT[0][:, :, 0:n].bitcast(fp32),
                                        ALU.subtract).then_inc(olo_done, 1)

            def add_products(h, c, which):
                for i in which:
                    t, half = c * (CW // P) + i // 2, i % 2
                    m = rows_of(t)
                    dve.wait_ge(g_ready, (h * NC + c) * NB + i + 1)
                    acc = rows[0:m, t, half * HALF:(half + 1) * HALF]
                    nc.vector.tensor_tensor(acc, acc, p_g[i % 2][0:m, 0:HALF], ALU.add).then_inc(g_out, 1)

            def score_rows(c):
                dve.wait_ge(a_in, 32)
                for t in range(c * (CW // P), (c + 1) * (CW // P)):
                    dve.wait_ge(g_out, (HEADS - 1) * NC * NB + t * 2 + 4)
                    for a in range(2):
                        if t >= 1:
                            dve.wait_ge(scored, 2 * (t - 1) + a + 1)
                        nc.vector.tensor_tensor_reduce(out=junk[:, a, :], in0=rows[:, t, :], in1=abc[:, a, :], scale=1.0,
                                                       scalar=0.0, op0=ALU.mult, op1=ALU.add,
                                                       accum_out=al[:, t, a * HEADS:a * HEADS + 1]).then_inc(scored, 1)

            def head(h):
                for c in range(NC):
                    q, last, second_last = h * NC + c, before(h, c, 1), before(h, c, 2)
                    for g in range(NG - 1):
                        wt.weigh(nc, dve, counts, q, c, g)
                        if g >= 1:
                            wt.lo(nc, dve, q, c, g - 1)
                        if c == 0 and 1 <= g <= 2:
                            split_rows(h, g - 1)
                    if last:
                        normalize(*last)
                    if second_last:
                        add_products(*second_last, range(2))
                    if c == 0:
                        split_rows(h, 2)
                    if last:
                        elu_in(*last)
                    if second_last:
                        add_products(*second_last, range(2, NB))
                    if c == 0:
                        split_rows(h, 3)
                    wt.weigh(nc, dve, counts, q, c, NG - 1)
                    wt.lo(nc, dve, q, c, NG - 2)
                    if last:
                        elu_out(*last)
                    wt.lo(nc, dve, q, c, NG - 1)
                    if c == 0:
                        split_rows(h, NG - 1)
                    if last:
                        elu_lo(*last)
                    if c == 1:
                        split_weights(h)
                    if is_final(h) and c >= 2:
                        score_rows(c - 2)

            head(0)
            with dve.Fori(1, HEADS - 1) as h:
                head(h)
            head(HEADS - 1)
            normalize(HEADS - 1, NC - 1)
            add_products(HEADS - 1, NC - 2, range(2))
            elu_in(HEADS - 1, NC - 1)
            add_products(HEADS - 1, NC - 2, range(2, NB))
            elu_out(HEADS - 1, NC - 1)
            elu_lo(HEADS - 1, NC - 1)
            score_rows(NC - 2)
            add_products(HEADS - 1, NC - 1, range(NB))
            score_rows(NC - 1)
            dve.wait_ge(scored, 2 * T)
            nc.vector.tensor_scalar(al02[:, :, 0:HEADS + 1], al[:, :, 0:HEADS + 1], SLOPE, None, ALU.mult).then_inc(scored, 1)
            dve.wait_ge(scored, 2 * T + 1)

        @block.tensor
        def _(pe):
            pe.sem_inc(wt.e_ready, 1)
            pe.sem_inc(wt.used, NG)

            def sums(h, c, final):
                n = CHUNKS[c][1]
                q = h * NC + c
                pe.wait_ge(z_done, q + 1)
                for s in range(T):
                    if s % G == 0:
                        pe.wait_ge(wt.lo_ready, q * NG + s // G + 1)
                    if c == 0:
                        pe.wait_ge(hlo_done, h * T + s + 1)
                    hi, lo = (wt.ring[a][:, s // G, s % G, 0:n] for a in range(2))
                    for f in range(KH):
                        cols = slice(f * P, (f + 1) * P)
                        for j, (a, r) in enumerate(((0, hi), (0, lo), (1, hi))):
                            nc.tensor.matmul(p_a[:, f, 0:n], hs[:, s, a, cols], r, start=s == 0 and j == 0,
                                             stop=s == T - 1 and j == 2)
                    for j, r in enumerate((hi, lo)):
                        last = nc.tensor.matmul(p_den[:, 0:n], ones_r[:, :], r, start=s == 0 and j == 0,
                                                stop=s == T - 1 and j == 1)
                    if s % G == G - 1:
                        last.then_inc(wt.used, 1)
                    if s == G - 1 and c + 1 < NC:
                        wt.broadcast(nc, pe, ident, shift_h[:, :], q + 1, c + 1)
                    if s == 2 * G - 1 and c == NC - 1 and not final:
                        pe.wait_ge(head_ready, h * 3 + 6)
                        wt.broadcast(nc, pe, ident, shift_h[:, :], q + 1, 0)

            def products(h, c):
                q = h * NC + c
                pe.wait_ge(olo_done, q + 1)
                if c == 0:
                    pe.wait_ge(wlo_done, h * KH + KH + 1)
                for i in range(NB):
                    dt, half = i // 2, i % 2
                    m = rows_of(c * (CW // P) + dt)
                    pe.wait_ge(g_out, q * NB + i + 1)
                    k_terms = [(k, a, b) for k in range(KH) for a, b in ((0, 0), (0, 1), (1, 0))]
                    for j, (k, a, b) in enumerate(k_terms):
                        last = nc.tensor.matmul(p_g[i % 2][0:m, 0:HALF], oT[a][:, k, dt * P:dt * P + m],
                                                w[b][:, k, half * HALF:(half + 1) * HALF], start=j == 0,
                                                stop=j == len(k_terms) - 1)
                    last.then_inc(g_ready, 1)

            def head(h):
                for c in range(NC):
                    second_last = before(h, c, 2)
                    if second_last:
                        products(*second_last)
                    sums(h, c, is_final(h))

            pe.wait_ge(head_ready, 3)
            wt.broadcast(nc, pe, ident, shift_h[:, :], 0, 0)
            head(0)
            with pe.Fori(1, HEADS - 1) as h:
                head(h)
            head(HEADS - 1)
            products(HEADS - 1, NC - 2)
            products(HEADS - 1, NC - 1)


def second_layer(nc, pool, st, x, b2, ident, counts, deg, dinv, al, al02, shiftT, rows, stats, mv):
    sb, pb, sem = pool(st)
    hs = [sb("hs2_hi", [P, T, AUG], f32r), sb("hs2_lo", [P, T, AUG], f32r)]
    bbc = sb("b2bc", [P, D], fp32)
    b_in, hi_done, lo_done, ones_done = (sem(n) for n in ("b2_in", "h2hi", "h2lo", "ones2"))

    def bias_beside(sp):
        sp.dma_start(bbc[:, :], b2.rearrange("(a n) -> a n", a=1).to_broadcast([P, D])).then_inc(b_in, 16)

    def hi_beside(act):
        for t in range(T):
            nc.scalar.activation(hs[0][:, t, 0:D], rows[:, t, :], ACT.Copy).then_inc(hi_done, 1)

    def ones_beside(pool_):
        nc.gpsimd.memset(hs[0][:, :, D:D + 2].bitcast(fp32), 1.0).then_inc(ones_done, 1)
        nc.gpsimd.memset(hs[0][:, :, D + 2:AUG].bitcast(fp32), 0.0).then_inc(ones_done, 1)
        nc.gpsimd.memset(hs[1][:, :, D:AUG].bitcast(fp32), 0.0).then_inc(ones_done, 1)

    shifts(nc, pool, 1, ident, counts, al, al02, shiftT, "two", bias_beside, hi_beside, ones_beside)

    wt = Weights(pool, st, "2")
    rden = sb("rden2", [P, CW // P], fp32)
    NDT = CW // P
    NPAIR = 3
    p_a = pb("p_a2", [P, NPAIR, 2, 512])
    x_in = [sem(f"x2_in{t}") for t in range(T)]
    pad_zero = sem("pad_zero2")
    biased = sem("biased")
    rden_done = sem("rden2_done")
    out_done = sem("out2_done")
    s_step = sem("s2_step")
    deg_root = sb("deg_root", [P, T], fp32)
    tmp = sb("tmp_d", [P, T], fp32)
    root_done = sem("root_done")
    with nc.Block() as block:
        @block.sync
        def _(sp):
            for t in range(T):
                sp.wait_ge(lo_done, t + 1)
                if t == T - 1:
                    sp.wait_ge(pad_zero, 1)
                sp.dma_start(rows[0:rows_of(t), t, :], x[t * P:t * P + rows_of(t), :]).then_inc(x_in[t], 16)

        @block.gpsimd
        def _(pool_):
            pool_.wait_ge(lo_done, T)
            nc.gpsimd.memset(rows[:, T - 1, :], 0.0).then_inc(pad_zero, 1)

        @block.scalar
        def _(act):
            for c in range(NC):
                for g in range(NG):
                    wt.exps(nc, act, (al[:, :, 0], al02[:, :, 0]), c, c, g)
                    if g >= 1:
                        wt.hi(nc, act, c, c, g - 1)
                wt.hi(nc, act, c, c, NG - 1)
            nc.scalar.activation(deg_root[:, :], deg[:, :], ACT.Sqrt).then_inc(root_done, 1)

        @block.vector
        def _(dve):
            chain = chain_on(dve, s_step)
            dve.sem_inc(wt.pf_ready, 2)
            dve.sem_inc(out_done, NPAIR)

            def split_rows(g):
                for t in range(g * G, (g + 1) * G):
                    nc.vector.tensor_tensor(hs[1][:, t, 0:D], rows[:, t, :], hs[0][:, t, 0:D].bitcast(fp32),
                                            ALU.subtract).then_inc(lo_done, 1)

            def residual(c):
                for t in range(c * NDT, (c + 1) * NDT):
                    m = rows_of(t)
                    dve.wait_ge(x_in[t], 16)
                    nc.vector.tensor_tensor(rows[0:m, t, :], rows[0:m, t, :], bbc[0:m, :], ALU.add).then_inc(biased, 1)

            def finish(c):
                dve.wait_ge(wt.used, (c + 2) * NG)
                for t in range(c * NDT, (c + 1) * NDT):
                    m = rows_of(t)
                    dt, pair = t % NDT, t % NPAIR
                    nc.vector.reciprocal(rden[0:m, dt:dt + 1], p_a[0:m, pair, 1, ONE:ONE + 1]).then_inc(rden_done, 1)
                    dve.wait_ge(rden_done, t + 1)
                    dve.wait_ge(biased, t + 1)
                    for half, (a, b) in enumerate(((0, AH), (AH, D))):
                        last = nc.vector.scalar_tensor_tensor(out=rows[0:m, t, a:b], in0=p_a[0:m, pair, half, 0:b - a],
                                                              scalar=rden[0:m, dt:dt + 1], in1=rows[0:m, t, a:b],
                                                              op0=ALU.mult, op1=ALU.add)
                    last.then_inc(out_done, 1)

            def statistics(c):
                for t in range(c * NDT, (c + 1) * NDT):
                    dve.wait_ge(out_done, NPAIR + t + 1)
                    row_stats(nc, chain, stats, mv, rows, t)

            for c in range(NC):
                for g in range(NG - 1):
                    wt.weigh(nc, dve, counts, c, c, g)
                    if g >= 1:
                        wt.lo(nc, dve, c, c, g - 1)
                    if c == 0:
                        split_rows(g)
                if c == 0:
                    split_rows(NG - 1)
                    dve.wait_ge(b_in, 16)
                else:
                    finish(c - 1)
                wt.weigh(nc, dve, counts, c, c, NG - 1)
                wt.lo(nc, dve, c, c, NG - 2)
                wt.lo(nc, dve, c, c, NG - 1)
                residual(c)
                if c >= 1:
                    statistics(c - 1)
            dve.wait_ge(root_done, 1)
            inverse_root(nc, chain, deg[:, :], deg_root[:, :], dinv[:, :], tmp[:, :])
            finish(NC - 1)
            statistics(NC - 1)

        @block.tensor
        def _(pe):
            pe.sem_inc(wt.e_ready, 1)
            pe.sem_inc(wt.used, NG)
            wt.broadcast(nc, pe, ident, shiftT[:, 0, :], 0, 0)
            for c in range(NC):
                for s in range(T):
                    if s % G == 0:
                        pe.wait_ge(wt.lo_ready, c * NG + s // G + 1)
                    if c == 0:
                        pe.wait_ge(lo_done, s + 1)
                    for dt in range(NDT):
                        t = c * NDT + dt
                        m = rows_of(t)
                        if s == 0:
                            pe.wait_ge(out_done, t + 1)
                        for half in range(2):
                            for j, (a, b) in enumerate(((0, 0), (0, 1), (1, 0))):
                                last = nc.tensor.matmul(p_a[0:m, t % NPAIR, half, 0:AH],
                                                        wt.ring[a][:, s // G, s % G, dt * P:dt * P + m],
                                                        hs[b][:, s, half * AH:(half + 1) * AH],
                                                        start=s == 0 and j == 0, stop=s == T - 1 and j == 2)
                    if s % G == G - 1:
                        last.then_inc(wt.used, 1)
                    if s == G - 1 and c + 1 < NC:
                        wt.broadcast(nc, pe, ident, shiftT[:, 0, :], c + 1, c + 1)


def convolutions(nc, pool, st, G1, c1, G2, c2, counts, dinv, rows, mv, g_scratch, out):
    sb, pb, sem = pool(st)
    hs = [sb("g_hi", [P, T, D], f32r), sb("g_lo", [P, T, D], f32r)]
    w = [sb("gw_hi", [P, KD, D], f32r), sb("gw_lo", [P, KD, D], f32r)]
    w_st = sb("gw_st", [P, 2, D], fp32)
    bbc = sb("gb", [P, 2, D], fp32)
    ve, root, rstd, nmr, tmp = (sb("g_" + n, [P, T], fp32) for n in ("ve", "root", "rstd", "nmr", "tmp"))
    hrow = sb("hrow", [P, 2, D], fp32)
    RS = 3
    ring = [sb("cr_hi", [P, RS, G, CW], f32r), sb("cr_lo", [P, RS, G, CW], f32r)]
    yT = [sb("yT_hi", [P, KD, CW], f32r), sb("yT_lo", [P, KD, CW], f32r)]
    orow = sb("orow", [P, 2, HALF], fp32)
    p_y = pb("p_y", [P, KD, 512])
    p_g = [pb("p_o0", [P, 512]), pb("p_o1", [P, 512])]
    b_in = sem("gb_in")
    w_in = [sem("gw_in0"), sem("gw_in1")]
    whi_done, wlo_done = sem("gwhi"), sem("gwlo")
    v_step, var_done, roots, norm_ready = sem("g_step"), sem("g_var"), sem("g_roots"), sem("g_norm")
    row_ready, hhi_done, hlo_done = sem("row_ready"), sem("ghi"), sem("glo")
    back_in = [sem(f"back_in{t}") for t in range(T)]
    chi_done, clo_done, used = sem("chi"), sem("clo"), sem("c_used")
    yhi_done, ylo_done = sem("yhi"), sem("ylo")
    g_ready, o_done, o_mid = sem("go_ready"), sem("go_done"), sem("go_mid")
    stored = [sem("stored0"), sem("stored1")]
    res_done = sem("res_done")
    NDT = CW // P
    NB = NDT * 2
    LAYERS = 2
    gview = [G1.rearrange("(k p) n -> p k n", p=P), G2.rearrange("(k p) n -> p k n", p=P)]

    with nc.Block() as block:
        @block.gpsimd
        def _(pool_):
            for l, b in enumerate((c1, c2)):
                pool_.dma_start(bbc[:, l, :], b.rearrange("(a n) -> a n", a=1).to_broadcast([P, D])).then_inc(b_in, 16)
            for l in range(LAYERS):
                for k in range(KD):
                    i = l * KD + k
                    if i >= 2:
                        pool_.wait_ge(wlo_done, i - 1)
                    pool_.dma_start(w_st[:, i % 2, :], gview[l][:, k, :]).then_inc(w_in[i % 2], 16)

        def row_back(sp, t):
            for j in range(2):
                sp.wait_ge(stored[j], 16 * (t + 1))
            sp.wait_ge(used, NC * NG)
            m = rows_of(t)
            sp.dma_start(hs[1][0:m, t, :].bitcast(fp32), g_scratch[t, 0:m, :]).then_inc(back_in[t], 16)

        @block.sync
        def _(sp):
            for l in range(LAYERS):
                for c in range(NC):
                    for i in range(NB):
                        n = (l * NC + c) * NB + i
                        t, half = c * NDT + i // 2, i % 2
                        m = rows_of(t)
                        cols = slice(half * HALF, (half + 1) * HALF)
                        sp.wait_ge(o_done, n + 1)
                        to = g_scratch[t, 0:m, cols] if l == 0 else out[t * P:t * P + m, cols]
                        sp.dma_start(to, orow[0:m, n % 2, :]).then_inc(stored[n % 2], 16)
                        if l == 0 and c == NC - 1 and i == 0:
                            for t in range(c * NDT):
                                row_back(sp, t)
                if l == 0:
                    for t in range((NC - 1) * NDT, T):
                        row_back(sp, t)
            for j in range(2):
                sp.wait_ge(stored[j], 16 * (LAYERS * NC * NB // 2))

        def w_terms():
            return [(k, a, b) for k in range(KD) for a, b in ((0, 0), (0, 1), (1, 0))]

        @block.scalar
        def _(act):
            def weight_hi(l, ks):
                for k in ks:
                    i = l * KD + k
                    act.wait_ge(w_in[i % 2], 16 * (i // 2 + 1))
                    if l == 1 and k == 0:
                        act.wait_ge(g_ready, NC * NB)
                    nc.scalar.activation(w[0][:, k, :], w_st[:, i % 2, :], ACT.Copy).then_inc(whi_done, 1)

            def count_hi(q, c, g):
                d0, n = CHUNKS[c]
                i = q * NG + g
                if i >= RS:
                    act.wait_ge(used, i - RS + 1)
                nc.scalar.activation(ring[0][:, i % RS, :, 0:n], counts[:, g * G:(g + 1) * G, d0:d0 + n],
                                     ACT.Copy).then_inc(chi_done, 1)

            act.wait_ge(var_done, 1)
            nc.scalar.activation(root[:, :], ve[:, :], ACT.Sqrt).then_inc(roots, 1)
            act.wait_ge(norm_ready, 1)
            def row_hi(l, t):
                m = rows_of(t)
                if l == 0:
                    m = P
                    if t >= 2:
                        act.wait_ge(hlo_done, t - 1)
                    nc.scalar.activation(hrow[:, t % 2, :], rows[:, t, :], ACT.Relu, bias=nmr[:, t:t + 1],
                                         scale=rstd[:, t:t + 1]).then_inc(row_ready, 1)
                    act.wait_ge(row_ready, t + 1)
                    full = hrow[:, t % 2, :]
                else:
                    act.wait_ge(back_in[t], 16)
                    full = hs[1][0:m, t, :].bitcast(fp32)
                nc.scalar.activation(hs[0][0:m, t, :], full, ACT.Copy).then_inc(hhi_done, 1)

            for l in range(LAYERS):
                for c in range(NC):
                    q = l * NC + c
                    for g in range(NG):
                        if c == 0:
                            for t in range(g * G, (g + 1) * G):
                                row_hi(l, t)
                        count_hi(q, c, g)
                        if c == 0 and l == 0:
                            weight_hi(l, (g,) if g < NG - 1 else range(g, KD))
                    if c == 0 and l == 1:
                        weight_hi(l, range(KD))
                    n = CHUNKS[c][1]
                    act.wait_ge(used, (q + 1) * NG)
                    if q >= 1:
                        act.wait_ge(g_ready, q * NB)
                    for f in range(KD):
                        nc.scalar.activation(yT[0][:, f, 0:n], p_y[:, f, 0:n], ACT.Copy).then_inc(yhi_done, 1)

        @block.vector
        def _(dve):
            chain = chain_on(dve, v_step)
            nc.vector.tensor_scalar(ve[:, :], mv[:, :, 1], EPS, None, ALU.add).then_inc(var_done, 1)
            dve.wait_ge(roots, 1)
            inverse_root(nc, chain, ve[:, :], root[:, :], rstd[:, :], tmp[:, :])
            chain(nc.vector.tensor_tensor(rstd[:, :], rstd[:, :], dinv[:, :], ALU.mult))
            nc.vector.scalar_tensor_tensor(out=nmr[:, :], in0=mv[:, :, 0], scalar=-1.0, in1=rstd[:, :],
                                           op0=ALU.mult, op1=ALU.mult).then_inc(norm_ready, 1)
            dve.wait_ge(b_in, 32)

            def weight_lo(l, ks):
                for k in ks:
                    i = l * KD + k
                    dve.wait_ge(whi_done, i + 1)
                    nc.vector.tensor_tensor(w[1][:, k, :], w_st[:, i % 2, :], w[0][:, k, :].bitcast(fp32),
                                            ALU.subtract).then_inc(wlo_done, 1)

            def count_lo(q, c, g):
                d0, n = CHUNKS[c]
                i = q * NG + g
                dve.wait_ge(chi_done, i + 1)
                nc.vector.tensor_tensor(ring[1][:, i % RS, :, 0:n], counts[:, g * G:(g + 1) * G, d0:d0 + n],
                                        ring[0][:, i % RS, :, 0:n].bitcast(fp32), ALU.subtract).then_inc(clo_done, 1)

            def row_lo(l, t):
                m = P if l == 0 else rows_of(t)
                dve.wait_ge(hhi_done, l * T + t + 1)
                full = hrow[:, t % 2, :] if l == 0 else hs[1][0:m, t, :].bitcast(fp32)
                nc.vector.tensor_tensor(hs[1][0:m, t, :], full, hs[0][0:m, t, :].bitcast(fp32), ALU.subtract).then_inc(hlo_done, 1)

            for l in range(LAYERS):
                for c in range(NC):
                    n = CHUNKS[c][1]
                    q = l * NC + c
                    for g in range(NG):
                        if c == 0:
                            for t in range(g * G, (g + 1) * G):
                                row_lo(l, t)
                        if c == 0 or g >= RS:
                            count_lo(q, c, g)
                        if c == 0 and l == 0:
                            weight_lo(l, (g,) if g < NG - 1 else range(g, KD))
                    if c == 0 and l == 1:
                        weight_lo(l, range(KD))
                    for f in range(KD):
                        dve.wait_ge(yhi_done, q * KD + f + 1)
                        nc.vector.tensor_tensor(yT[1][:, f, 0:n], p_y[:, f, 0:n], yT[0][:, f, 0:n].bitcast(fp32),
                                                ALU.subtract).then_inc(ylo_done, 1)
                    if c + 1 < NC:
                        for g in range(RS):
                            count_lo(q + 1, c + 1, g)
                    if l == 0:
                        for t in range(c * NDT, (c + 1) * NDT):
                            nc.vector.tensor_tensor(rows[:, t, :], rows[:, t, :], bbc[:, 1, :], ALU.add).then_inc(res_done, 1)
                    for i in range(NB):
                        j = q * NB + i
                        t, half = c * NDT + i // 2, i % 2
                        m = rows_of(t)
                        cols = slice(half * HALF, (half + 1) * HALF)
                        dve.wait_ge(g_ready, j + 1)
                        if j >= 2:
                            dve.wait_ge(stored[j % 2], 16 * (j // 2))
                        o = orow[0:m, j % 2, :]
                        dv = dinv[0:m, t:t + 1]
                        if l == 0:
                            nc.vector.scalar_tensor_tensor(out=o, in0=p_g[i % 2][0:m, 0:HALF], scalar=dv, in1=bbc[0:m, 0, cols],
                                                           op0=ALU.mult, op1=ALU.add).then_inc(o_mid, 1)
                            dve.wait_ge(o_mid, j + 1)
                            nc.vector.tensor_scalar(o, o, 0.0, dv, ALU.max, ALU.mult).then_inc(o_done, 1)
                        else:
                            dve.wait_ge(res_done, T)
                            nc.vector.scalar_tensor_tensor(out=o, in0=p_g[i % 2][0:m, 0:HALF], scalar=dv, in1=rows[0:m, t, cols],
                                                           op0=ALU.mult, op1=ALU.add).then_inc(o_done, 1)

        @block.tensor
        def _(pe):
            for l in range(LAYERS):
                for c in range(NC):
                    n = CHUNKS[c][1]
                    q = l * NC + c
                    if q >= 1:
                        pe.wait_ge(ylo_done, q * KD)
                    for s in range(T):
                        i = q * NG + s // G
                        if s % G == 0:
                            pe.wait_ge(clo_done, i + 1)
                        if c == 0:
                            pe.wait_ge(hlo_done, l * T + s + 1)
                        hi, lo = (ring[a][:, i % RS, s % G, 0:n] for a in range(2))
                        for f in range(KD):
                            cols = slice(f * P, (f + 1) * P)
                            for j, (a, r) in enumerate(((0, hi), (0, lo), (1, hi))):
                                last = nc.tensor.matmul(p_y[:, f, 0:n], hs[a][:, s, cols], r, start=s == 0 and j == 0,
                                                        stop=s == T - 1 and j == 2)
                        if s % G == G - 1:
                            last.then_inc(used, 1)
                    for i in range(NB):
                        j = q * NB + i
                        dt, half = i // 2, i % 2
                        m = rows_of(c * NDT + dt)
                        if j >= 2:
                            pe.wait_ge(o_done, j - 1)
                        terms = w_terms()
                        for u, (k, a, b) in enumerate(terms):
                            if i == 0 and u % 3 == 0:
                                pe.wait_ge(ylo_done, q * KD + k + 1)
                                if c == 0:
                                    pe.wait_ge(wlo_done, l * KD + k + 1)
                            last = nc.tensor.matmul(p_g[i % 2][0:m, 0:HALF], yT[a][:, k, dt * P:dt * P + m],
                                                    w[b][:, k, half * HALF:(half + 1) * HALF], start=u == 0,
                                                    stop=u == len(terms) - 1)
                        last.then_inc(g_ready, 1)


_INPUTS = ["x", "src", "dst", "L0_gnn_W1", "L0_gnn_att_src1", "L0_gnn_att_dst1", "L0_gnn_b1", "L0_gnn_W2",
           "L0_gnn_att_src2", "L0_gnn_att_dst2", "L0_gnn_b2", "L1_gnn_W1", "L1_gnn_b1", "L1_gnn_W2", "L1_gnn_b2"]


def kernel(**inputs):
    import numpy as np
    import concourse.bacc as bacc
    from concourse.bass_utils import run_bass_kernel_spmd as run

    nc = bacc.Bacc("TRN2", target_bir_lowering=False, num_devices=1)
    arrays, args = {}, []
    for name in _INPUTS:
        a = np.ascontiguousarray(inputs[name])
        arrays["in_" + name] = a
        args.append(nc.dram_tensor("in_" + name, a.shape, mybir.dt.from_np(a.dtype), kind="ExternalInput").ap())
    args.append(nc.dram_tensor("out_nodes", (N, D), fp32, kind="ExternalOutput").ap())
    build(nc, *args)
    r = run(nc, [arrays], core_ids=[0])
    return r.results[0]["out_nodes"]
```
